# Optimizing a Trainium2 kernel written in Bass

```python
import numpy as np
import jax
import jax.numpy as jnp

def _softmax(x, axis=-1):
    return jax.nn.softmax(x, axis=axis)

def _gelu(x):
    return jax.nn.gelu(x, approximate=True)

def _silu(x):
    return jax.nn.silu(x)

def _sigmoid(x):
    return jax.nn.sigmoid(x)

def _layernorm(x, axis=-1, eps=1e-05):
    m = jnp.mean(x, axis=axis, keepdims=True)
    v = jnp.var(x, axis=axis, keepdims=True)
    return (x - m) / jnp.sqrt(v + eps)

def _scatter_add(tgt, idx, src, axis=0):
    return tgt.at[idx].add(src)

def _segment_sum(src, seg, n):
    return jax.ops.segment_sum(src, seg, n)
kernel_name = 'mk_rec_standalone_d1_rec_r8_9939aa'

def setup_inputs(seed: int=0):
    np.random.seed(seed)
    _w = jnp.asarray

    def _rec_inputs():
        import jax
        import jax.numpy as jnp
        _rk = jax.random.key(seed)
        r_x_dense = -0.00338568 + 1.0005 * jax.random.normal(jax.random.fold_in(_rk, 1), (1024, 13), jnp.float32)
        r_x_sparse = jnp.stack([jax.random.randint(jax.random.fold_in(jax.random.fold_in(_rk, 2), 0), (1024,), 6, 49999, jnp.int32), jax.random.randint(jax.random.fold_in(jax.random.fold_in(_rk, 2), 1), (1024,), 4, 49989, jnp.int32), jax.random.randint(jax.random.fold_in(jax.random.fold_in(_rk, 2), 2), (1024,), 0, 49999, jnp.int32), jax.random.randint(jax.random.fold_in(jax.random.fold_in(_rk, 2), 3), (1024,), 0, 49991, jnp.int32), jax.random.randint(jax.random.fold_in(jax.random.fold_in(_rk, 2), 4), (1024,), 1, 49996, jnp.int32), jax.random.randint(jax.random.fold_in(jax.random.fold_in(_rk, 2), 5), (1024,), 1, 6250, jnp.int32), jax.random.randint(jax.random.fold_in(jax.random.fold_in(_rk, 2), 6), (1024,), 0, 49994, jnp.int32), jax.random.randint(jax.random.fold_in(jax.random.fold_in(_rk, 2), 7), (1024,), 6, 49999, jnp.int32), jax.random.randint(jax.random.fold_in(jax.random.fold_in(_rk, 2), 8), (1024,), 0, 6250, jnp.int32), jax.random.randint(jax.random.fold_in(jax.random.fold_in(_rk, 2), 9), (1024,), 5, 49999, jnp.int32), jax.random.randint(jax.random.fold_in(jax.random.fold_in(_rk, 2), 10), (1024,), 2, 49994, jnp.int32), jax.random.randint(jax.random.fold_in(jax.random.fold_in(_rk, 2), 11), (1024,), 5, 49997, jnp.int32), jax.random.randint(jax.random.fold_in(jax.random.fold_in(_rk, 2), 12), (1024,), 0, 49999, jnp.int32), jax.random.randint(jax.random.fold_in(jax.random.fold_in(_rk, 2), 13), (1024,), 1, 49998, jnp.int32), jax.random.randint(jax.random.fold_in(jax.random.fold_in(_rk, 2), 14), (1024,), 1, 49994, jnp.int32), jax.random.randint(jax.random.fold_in(jax.random.fold_in(_rk, 2), 15), (1024,), 2, 6250, jnp.int32), jax.random.randint(jax.random.fold_in(jax.random.fold_in(_rk, 2), 16), (1024,), 4, 49999, jnp.int32), jax.random.randint(jax.random.fold_in(jax.random.fold_in(_rk, 2), 17), (1024,), 0, 6250, jnp.int32), jax.random.randint(jax.random.fold_in(jax.random.fold_in(_rk, 2), 18), (1024,), 1, 49998, jnp.int32), jax.random.randint(jax.random.fold_in(jax.random.fold_in(_rk, 2), 19), (1024,), 1, 49998, jnp.int32), jax.random.randint(jax.random.fold_in(jax.random.fold_in(_rk, 2), 20), (1024,), 2, 49998, jnp.int32), jax.random.randint(jax.random.fold_in(jax.random.fold_in(_rk, 2), 21), (1024,), 2, 49995, jnp.int32), jax.random.randint(jax.random.fold_in(jax.random.fold_in(_rk, 2), 22), (1024,), 3, 49998, jnp.int32), jax.random.randint(jax.random.fold_in(jax.random.fold_in(_rk, 2), 23), (1024,), 2, 49997, jnp.int32), jax.random.randint(jax.random.fold_in(jax.random.fold_in(_rk, 2), 24), (1024,), 9, 6250, jnp.int32), jax.random.randint(jax.random.fold_in(jax.random.fold_in(_rk, 2), 25), (1024,), 2, 49993, jnp.int32)], axis=1)
        return (r_x_dense, r_x_sparse)
    r_x_dense, r_x_sparse = _rec_inputs()

    def _L0_rec_setup():
        import jax, jax.numpy as jnp
        import numpy as np
        N_DENSE = 13
        N_FIELDS = 26
        VOCAB = 6250
        K = 64
        BATCH = 2048
        HID = N_FIELDS * (N_FIELDS - 1) // 2 + N_FIELDS * K + N_DENSE
        key = jax.random.key(seed)
        ks = jax.random.split(key, 7)
        x_dense = jax.random.normal(ks[0], (BATCH, N_DENSE), dtype=jnp.float32)
        x_sparse = jax.random.randint(ks[1], (BATCH, N_FIELDS), 0, VOCAB)
        lim_e = np.sqrt(6.0 / (VOCAB + K))
        emb_tables = jax.random.uniform(ks[2], (N_FIELDS, VOCAB, K), minval=-lim_e, maxval=lim_e, dtype=jnp.float32)
        lim1 = np.sqrt(1.0 / HID)
        w1 = jax.random.uniform(ks[3], (HID, HID), minval=-lim1, maxval=lim1, dtype=jnp.float32)
        b1 = jax.random.uniform(ks[4], (HID,), minval=-lim1, maxval=lim1, dtype=jnp.float32)
        w2 = jax.random.uniform(ks[5], (HID, 1), minval=-lim1, maxval=lim1, dtype=jnp.float32)
        b2 = jax.random.uniform(ks[6], (1,), minval=-lim1, maxval=lim1, dtype=jnp.float32)
        return {'x_dense': x_dense, 'x_sparse': x_sparse, 'emb_tables': emb_tables, 'w1': w1, 'b1': b1, 'w2': w2, 'b2': b2}
    _L0_rec_all = _L0_rec_setup()
    _L0_rec_in = {k: v for k, v in _L0_rec_all.items() if k in ('emb_tables', 'w1', 'b1', 'w2', 'b2')}
    del _L0_rec_all
    return {'r_x_dense': r_x_dense, 'r_x_sparse': r_x_sparse, 'L0_rec_emb_tables': _L0_rec_in['emb_tables'], 'L0_rec_w1': _L0_rec_in['w1'], 'L0_rec_b1': _L0_rec_in['b1'], 'L0_rec_w2': _L0_rec_in['w2'], 'L0_rec_b2': _L0_rec_in['b2']}

def reference(r_x_dense, r_x_sparse, L0_rec_emb_tables, L0_rec_w1, L0_rec_b1, L0_rec_w2, L0_rec_b2):
    import jax
    import jax.numpy as jnp

    def _L0_rec_ref(x_dense, x_sparse, emb_tables, w1, b1, w2, b2):
        import jax, jax.numpy as jnp
        import numpy as np
        N_DENSE = 13
        N_FIELDS = 26
        VOCAB = 6250
        K = 64
        BATCH = 2048
        HID = N_FIELDS * (N_FIELDS - 1) // 2 + N_FIELDS * K + N_DENSE
        B = x_dense.shape[0]
        field_idx = jnp.arange(N_FIELDS)
        sparse_embed = emb_tables[field_idx[None, :], x_sparse]
        z = sparse_embed.reshape(B, N_FIELDS * K)
        gram = jnp.einsum('bik,bjk->bij', sparse_embed, sparse_embed)
        iu, ju = jnp.triu_indices(N_FIELDS, k=1)
        inner = gram[:, iu, ju]
        dnn_in = jnp.concatenate([x_dense, z, inner], axis=-1)
        h = jax.nn.relu(dnn_in @ w1 + b1)
        out = jax.nn.sigmoid(h @ w2 + b2)
        return out
    y = _L0_rec_ref(r_x_dense, r_x_sparse, L0_rec_emb_tables, L0_rec_w1, L0_rec_b1, L0_rec_w2, L0_rec_b2)
    return y

_drawn_inputs = setup_inputs


def setup_inputs(seed=0):
    import zlib

    import numpy as np

    out = dict(_drawn_inputs(seed))
    spreads = {}
    factors = {'r_x_dense': 5.385,
     'L0_rec_emb_tables': 8.0,
     'L0_rec_w1': 6.286,
     'L0_rec_b1': 8.0,
     'L0_rec_w2': 7.992}
    for name, (base, spread) in spreads.items():
        noise = np.random.default_rng([zlib.crc32(name.encode()), seed]).standard_normal(out[name].shape)
        drawn = base * np.exp(spread * noise) if base else spread * noise
        out[name] = jnp.asarray(drawn.astype(out[name].dtype))
    for name, factor in factors.items():
        out[name] = (out[name] * factor).astype(out[name].dtype)
    return out
```

```python
import concourse.bass as bass
from concourse import mybir
from contextlib import ExitStack


def product_interaction_mlp_kernel(nc, x_dense, x_sparse, emb, w1, b1, w2, b2, out):
    fp32 = mybir.dt.float32
    f32r = mybir.dt.float32r
    i32 = mybir.dt.int32
    ALU = mybir.AluOpType
    ACT = mybir.ActivationFunctionType
    AX = mybir.AxisListType

    P = 128
    BATCH, DENSE = x_dense.shape
    FIELDS, VOCAB, K = emb.shape
    HID = w1.shape[0]
    TILES = BATCH // P
    GROUP = 2
    PAIRS = FIELDS * (FIELDS - 1) // 2
    FP = FIELDS // 2
    TAIL = PAIRS + DENSE + 1
    TT = -(-TAIL // P)
    KT = FP + TT
    LAST = TAIL - (TT - 1) * P
    HALVES = 2
    CW = [502, 500]
    HW = sum(CW)
    HSTEP = HID - HW
    BATCHES = [(0, 3), (3, 4), (7, 4), (11, FP - 11)]
    GB = 16
    GBANKS = P // GB
    RAW = 4
    SPL = 6
    LEAD = 4
    XS = 4
    RR = FIELDS // 2

    STEPS = HALVES * TILES // GROUP

    TURN = [(0, k, [t]) for t in range(GROUP) for k in range(FP)]
    TURN += [(0, k, list(range(GROUP))) for k in range(FP, KT)]
    for n in range(1, STEPS):
        TURN += [(n, k, [n // HALVES * GROUP + b for b in range(GROUP)]) for k in range(KT)]
    TURNS = len(TURN)

    AFTER = {}
    for t, ts, os, gs, r, x in [
            (0, [-1, 2, 6, 10], [0, 3, 7, 10], [12, 12, 12, 13, 13, 13, 13, 13], 14, 15),
            (1, [12, 14, 18, 21], [15, 16, 19, 21], [22, 22, 23, 23, 24, 24, 24, 24], 25, 25),
            (2, [25, 27, 29, 31], [26, 28, 30, 32], [33, 33, 34, 34, 35, 35, 36, 36], 37, 38),
            (3, [39, 40, 42, 44], [40, 41, 43, 45], [46, 46, 47, 47, 48, 48, 49, 49], 50, 51),
            (4, [52, 54, 56, 58], [53, 55, 57, 59], [60, 60, 61, 61, 62, 62, 63, 63], 64, 65),
            (5, [66, 68, 70, 72], [67, 69, 71, 73], [74, 74, 75, 75, 76, 76, 77, 77], 78, 79),
            (6, [80, 82, 84, 86], [81, 83, 85, 87], [88, 88, 89, 89, 90, 90, 91, 91], 92, 93),
            (7, [95, 97, 99, 101], [96, 98, 100, 102], [103, 103, 104, 104, 105, 105, 106, 106], 107, 108)]:
        for kind, turns in (("T", ts), ("O", os), ("G", gs), ("R", [r]), ("X", [x])):
            for q, u in enumerate(turns):
                AFTER.setdefault(u, []).append((kind, t, q))
    FIRST = min(AFTER)
    ORDER = [e for u in sorted(AFTER) for e in AFTER[u]]

    def count(kinds, event):
        return sum(e[0] in kinds for e in ORDER[:ORDER.index(event) + 1])

    USES = [(*e, j) for e in ORDER if e[0] in "TXR" for j in range(2 if e[0] == "R" else 1)]

    def bank(event, j=0):
        return USES.index((*event, j)) % 2

    emb_rows = emb.rearrange("f v k -> (f v) k")

    def row_of(i):
        return sum(FIELDS - 1 - m for m in range(i))

    with ExitStack() as ctx:
        def sb(name, shape, dt):
            return ctx.enter_context(nc.sbuf_tensor(name, shape, dt))

        def pb(name):
            return ctx.enter_context(nc.psum_tensor(name, [P, 512], fp32))

        def sem(name):
            return ctx.enter_context(nc.semaphore(name))

        idx = sb("idx", [P, TILES, FIELDS], i32)
        wrap = sb("wrap", [P, TILES, FIELDS], i32)
        base = sb("base", [P, TILES, FIELDS], i32)
        ident = sb("ident", [P, P], fp32)
        dense = sb("dense", [P, TILES, DENSE], fp32)
        w2b = sb("w2b", [P, HALVES, HW], fp32)
        b2b = sb("b2b", [TILES, 1], fp32)
        z = sb("z", [P, 2, FIELDS * K], fp32)
        x_hi = sb("x_hi", [P, XS, KT, P], f32r)
        x_lo = sb("x_lo", [P, XS, KT, P], f32r)
        pair_u = sb("pair_u", [P, FIELDS, P], f32r)
        pair_v = sb("pair_v", [P, FIELDS, P], f32r)
        gram = sb("gram", [FIELDS, P, FIELDS], fp32)
        square = sb("square", [P, FIELDS, FIELDS], fp32)
        tail = sb("tail", [P, TT * P], fp32)
        w_raw = sb("w_raw", [P, RAW, HW], fp32)
        w_hi = sb("w_hi", [P, SPL, HW], f32r)
        w_lo = sb("w_lo", [P, SPL, HW], f32r)
        weighed = sb("weighed", [P, 2, 512], fp32)
        parts = sb("parts", [P, TILES * 2 * HALVES], fp32)
        logits = sb("logits", [P, TILES], fp32)
        y = sb("y", [TILES, P], fp32)

        acc = [pb(f"acc{j}") for j in range(4)]
        ps_x = [pb(f"ps_x{j}") for j in range(2)]
        ps_g = [pb(f"ps_g{j}") for j in range(2)]

        idx_in = sem("idx_in")
        dense_in = sem("dense_in")
        w2_in = sem("w2_in")
        b2_in = sem("b2_in")
        w_in = [sem(f"w_in{j}") for j in range(RAW)]
        base_done = sem("base_done")
        ident_zero = sem("ident_zero")
        ident_done = sem("ident_done")
        idx_step = sem("idx_step")
        idx_done = sem("idx_done")
        w2_zero = sem("w2_zero")
        gathered = [[sem(f"gathered{z}_{q}") for q in range(len(BATCHES))] for z in range(2)]
        transposed = sem("transposed")
        x_hi_done = sem("x_hi_done")
        x_lo_done = sem("x_lo_done")
        pairs_act = sem("pairs_act")
        pairs_dve = sem("pairs_dve")
        gram_made = sem("gram_made")
        gram_act = sem("gram_act")
        gram_dve = sem("gram_dve")
        rows_made = sem("rows_made")
        rows_done = sem("rows_done")
        tail_done = sem("tail_done")
        w_hi_done = sem("w_hi_done")
        w_lo_done = sem("w_lo_done")
        w_used = sem("w_used")
        acc_made = sem("acc_made")
        acc_read = sem("acc_read")
        sum_done = sem("sum_done")
        y_made = sem("y_made")
        y_done = sem("y_done")
        out_done = sem("out_done")

        block = ctx.enter_context(nc.Block())

        def ahead(u):
            return [m for m in range(2, TURNS) if max(m - LEAD, 0) == u]

        def last_of(n):
            return max(u for u in range(TURNS) if TURN[u][0] == n)

        def gram_counts(n):
            return (n + 1) // 2, n // 2

        def raw_count(m):
            return 16 * sum(3 if TURN[i][1] == KT - 1 else 1 for i in range(m % RAW, m + 1, RAW))

        @block.sync
        def _(sp):
            sp.dma_start(idx[:], x_sparse.rearrange("(t p) f -> p t f", p=P)).then_inc(idx_in, 16)

            def load_piece(m):
                k, h = TURN[m][1], TURN[m][0] % HALVES
                cols, slot = slice(h * HSTEP, h * HSTEP + HW), m % RAW
                if m >= RAW:
                    sp.wait_ge(w_lo_done, m - RAW + 1)
                if k < KT - 1:
                    r = DENSE + P * k
                    sp.dma_start(w_raw[:, slot, :], w1[r:r + P, cols]).then_inc(w_in[slot], 16)
                else:
                    n = PAIRS - (TT - 1) * P
                    sp.dma_start(w_raw[0:n, slot, :], w1[HID - n:HID, cols]).then_inc(w_in[slot], 16)
                    sp.dma_start(w_raw[n:n + DENSE, slot, :], w1[0:DENSE, cols]).then_inc(w_in[slot], 16)
                    sp.dma_start(w_raw[n + DENSE:LAST, slot, :],
                                 b1[cols].unsqueeze(0)).then_inc(w_in[slot], 16)

            for m in range(LEAD):
                if m >= 2:
                    sp.wait_ge(w_lo_done, m - 1)
                load_piece(m)
            sp.dma_start(dense[:], x_dense.rearrange("(t p) d -> p t d", p=P)).then_inc(dense_in, 16)
            sp.wait_ge(w2_zero, 1)
            for h in range(HALVES):
                o = 2 if h else 0
                sp.dma_start(w2b[:, h, o:HW],
                             w2[h * HSTEP + o:h * HSTEP + HW, :].rearrange("n o -> o n")
                             .broadcast_to([P, HW - o])).then_inc(w2_in, 16)
            sp.dma_start(b2b[:], b2.unsqueeze(0).broadcast_to([TILES, 1])).then_inc(b2_in, 16)
            for m in range(LEAD, TURNS):
                load_piece(m)
            sp.wait_ge(y_done, 1)
            sp.dma_start(out.rearrange("(t p) o -> t (p o)", p=P), y[:]).then_inc(out_done, 16)
            sp.wait_ge(out_done, 16)

        @block.gpsimd
        def _(pool):
            nc.gpsimd.iota(base[:], pattern=[[0, TILES], [VOCAB, FIELDS]], base=0,
                           channel_multiplier=0).then_inc(base_done, 1)
            nc.gpsimd.memset(ident[:], 0.0).then_inc(ident_zero, 1)
            pool.wait_ge(ident_zero, 1)
            nc.gpsimd.affine_select(out=ident[:], in_=ident[:], compare_op=ALU.not_equal, fill=1.0, base=0,
                                    pattern=[[-1, P]], channel_multiplier=1).then_inc(ident_done, 1)
            pool.wait_ge(idx_done, 1)
            for t in range(TILES):
                for q, (first, n) in enumerate(BATCHES):
                    if t >= 2:
                        pool.wait_ge(transposed, count("TX", ("T", t - 2, q)))
                    for f in range(2 * first, 2 * (first + n)):
                        pool.indirect_dma_start(
                            out=z[:, t % 2, K * f:K * (f + 1)], out_offset=None, in_=emb_rows,
                            in_offset=bass.IndirectOffsetOnAxis(ap=idx[:, t, f:f + 1], axis=0),
                        ).then_inc(gathered[t % 2][q], 16)

        @block.tensor
        def _(pe):
            def bank_free(event, j=0):
                u = USES.index((*event, j))
                if u >= 2:
                    kind, t, q, i = USES[u - 2]
                    if kind == "R":
                        pe.wait_ge(rows_done, 2 * count("R", (kind, t, q)) - 1 + i)
                    else:
                        pe.wait_ge(x_lo_done, count("TX", (kind, t, q)))

            def transpose_z(t, q):
                first, n = BATCHES[q]
                pe.wait_ge(gathered[t % 2][q], 16 * 2 * n * (t // 2 + 1))
                bank_free(("T", t, q))
                for j in range(n):
                    last = nc.tensor.transpose(ps_x[bank(("T", t, q))][:, P * j:P * (j + 1)],
                                               z[:, t % 2, P * (first + j):P * (first + j + 1)], ident[:])
                last.then_inc(transposed, 1)

            def pair_products(t, q):
                if q == 0:
                    pe.wait_ge(pairs_act, len(BATCHES) * (t + 1))
                    pe.wait_ge(pairs_dve, len(BATCHES) * (t + 1))
                n = GBANKS * t + q
                if n >= 2:
                    pe.wait_ge(*((gram_dve, gram_counts(n - 1)[1]) if n % 2 else
                                 (gram_act, gram_counts(n - 1)[0])))
                for g in range(GB):
                    s = GB * q + g
                    last = nc.tensor.matmul(ps_g[q % 2][0:FIELDS, g * FIELDS:(g + 1) * FIELDS],
                                            pair_u[:, :, s], pair_v[:, :, s], start=True, stop=True)
                last.then_inc(gram_made, 1)

            def product_rows(t):
                pe.wait_ge(gram_act, gram_counts(GBANKS * (t + 1))[0])
                pe.wait_ge(gram_dve, gram_counts(GBANKS * (t + 1))[1])
                for j in range(2):
                    bank_free(("R", t, 0), j)
                    for i in range(RR):
                        last = nc.tensor.transpose(
                            ps_x[bank(("R", t, 0), j)][:, FIELDS * i:FIELDS * (i + 1)],
                            gram[:, :, RR * j + i], ident[0:FIELDS, 0:FIELDS])
                    last.then_inc(rows_made, 1)

            def transpose_tail(t):
                pe.wait_ge(tail_done, t + 1)
                bank_free(("X", t, 0))
                for j in range(TT):
                    last = nc.tensor.transpose(ps_x[bank(("X", t, 0))][:, P * j:P * (j + 1)],
                                               tail[:, P * j:P * (j + 1)], ident[:])
                last.then_inc(transposed, 1)

            def multiply(m):
                (n, k, tiles), slot = TURN[m], m % SPL
                rows = LAST if k == KT - 1 else P
                for q, (first, _) in enumerate(BATCHES):
                    if k == first:
                        pe.wait_ge(x_lo_done, count("TX", ("T", tiles[-1], q)))
                if k == FP:
                    pe.wait_ge(x_lo_done, count("TX", ("X", tiles[-1], 0)))
                pe.wait_ge(w_hi_done, m + 1)
                pe.wait_ge(w_lo_done, m + 1)
                for c, w in enumerate(CW):
                    cols = slice(sum(CW[:c]), sum(CW[:c]) + w)
                    for t in tiles:
                        j, x = GROUP * c + t % GROUP, t % XS
                        if k == 0 and n >= 1:
                            pe.wait_ge(acc_read, len(acc) * (n - 1) + j + 1)
                        o = acc[j][:, 0:w]
                        hi, lo = x_hi[0:rows, x, k, :], x_lo[0:rows, x, k, :]
                        nc.tensor.matmul(o, hi, w_hi[0:rows, slot, cols], start=k == 0, stop=False)
                        nc.tensor.matmul(o, hi, w_lo[0:rows, slot, cols], start=False, stop=False)
                        last = nc.tensor.matmul(o, lo, w_hi[0:rows, slot, cols], start=False,
                                                stop=k == KT - 1)
                        if k == KT - 1 and j < len(acc) - 1:
                            last.then_inc(acc_made, 1)
                last.then_inc(w_used, 1)

            PARTS = {"T": transpose_z, "G": pair_products, "R": lambda t, _: product_rows(t),
                     "X": lambda t, _: transpose_tail(t), "O": lambda t, q: None}
            pe.wait_ge(ident_done, 1)
            for u in range(FIRST, TURNS):
                if u >= 0:
                    multiply(u)
                for kind, t, q in AFTER.get(u, []):
                    PARTS[kind](t, q)
            pe.wait_ge(sum_done, 1)
            nc.tensor.transpose(ps_x[0][0:TILES, 0:P], logits[:], ident[:]).then_inc(y_made, 1)

        @block.scalar
        def _(act):
            def split_piece(m):
                slot = m % SPL
                rows = LAST if TURN[m][1] == KT - 1 else P
                act.wait_ge(w_in[m % RAW], raw_count(m))
                if m >= SPL:
                    act.wait_ge(w_used, m - SPL + 1)
                nc.scalar.copy(w_hi[0:rows, slot, :], w_raw[0:rows, m % RAW, :]).then_inc(w_hi_done, 1)

            def high_z(t, q):
                first, n = BATCHES[q]
                act.wait_ge(transposed, count("TX", ("T", t, q)))
                nc.scalar.copy(x_hi[:, t % XS, first:first + n, :].rearrange("p k b -> p (k b)"),
                               ps_x[bank(("T", t, q))][:, 0:n * P]).then_inc(x_hi_done, 1)

            def pair_operands(t, q):
                first, n = BATCHES[q]
                if q == 0 and t >= 1:
                    act.wait_ge(gram_made, GBANKS * t)
                act.wait_ge(x_hi_done, count("TX", ("T", t, q)))
                for par in range(2):
                    f = slice(2 * first + par, 2 * (first + n), 2)
                    high = x_hi[K * par:K * (par + 1), t % XS, first:first + n, :].bitcast(fp32)
                    nc.scalar.mul(pair_v[0:K, f, :], high, 0.5)
                    last = nc.scalar.copy(pair_u[0:K, f, :], high)
                last.then_inc(pairs_act, 1)

            def read_pairs(t, q):
                if q % 2 == 0:
                    act.wait_ge(gram_made, GBANKS * t + q + 1)
                    nc.scalar.copy(gram[:, GB * q:GB * (q + 1), :].rearrange("i b j -> i (b j)"),
                                   ps_g[q % 2][0:FIELDS, 0:GB * FIELDS]).then_inc(gram_act, 1)

            def read_rows(t):
                for j in range(2):
                    act.wait_ge(rows_made, 2 * t + j + 1)
                    nc.scalar.copy(square[:, RR * j:RR * (j + 1), :].rearrange("p i j -> p (i j)"),
                                   ps_x[bank(("R", t, 0), j)][:, 0:RR * FIELDS]).then_inc(rows_done, 1)

            def high_tail(t):
                act.wait_ge(transposed, count("TX", ("X", t, 0)))
                nc.scalar.copy(x_hi[:, t % XS, FP:KT, :].rearrange("p k b -> p (k b)"),
                               ps_x[bank(("X", t, 0))][:, 0:TT * P]).then_inc(x_hi_done, 1)

            PARTS = {"T": high_z, "O": pair_operands, "G": read_pairs, "R": lambda t, _: read_rows(t),
                     "X": lambda t, _: high_tail(t)}
            for m in range(2):
                split_piece(m)
            for u in range(FIRST, TURNS):
                for m in ahead(u):
                    split_piece(m)
                for kind, t, q in AFTER.get(u, []):
                    PARTS[kind](t, q)
            act.wait_ge(b2_in, 16)
            act.wait_ge(y_made, 1)
            nc.scalar.activation(y[:], ps_x[0][0:TILES, 0:P], ACT.Sigmoid, bias=b2b[:]).then_inc(y_done, 1)

        @block.vector
        def _(dve):
            dve.wait_ge(idx_in, 16)
            nc.vector.tensor_scalar(wrap[:], idx[:], 0, VOCAB, ALU.is_lt, ALU.mult).then_inc(idx_step, 1)
            dve.wait_ge(idx_step, 1)
            nc.vector.tensor_tensor(idx[:], idx[:], wrap[:], ALU.add).then_inc(idx_step, 1)
            dve.wait_ge(idx_step, 2)
            nc.vector.tensor_scalar(idx[:], idx[:], VOCAB - 1, 0, ALU.min, ALU.max).then_inc(idx_step, 1)
            dve.wait_ge(idx_step, 3)
            dve.wait_ge(base_done, 1)
            nc.vector.tensor_tensor(idx[:], idx[:], base[:], ALU.add).then_inc(idx_done, 1)
            nc.vector.memset(tail[:, TAIL:TT * P], 0.0)
            nc.vector.memset(tail[:, TAIL - 1:TAIL], 1.0)
            nc.vector.memset(w2b[:, 1, 0:2], 0.0).then_inc(w2_zero, 1)

            def split_piece(m):
                slot = m % SPL
                rows = LAST if TURN[m][1] == KT - 1 else P
                dve.wait_ge(w_hi_done, m + 1)
                nc.vector.tensor_tensor(w_lo[0:rows, slot, :], w_raw[0:rows, m % RAW, :],
                                        w_hi[0:rows, slot, :], ALU.subtract).then_inc(w_lo_done, 1)

            def low_z(t, q):
                first, n = BATCHES[q]
                flat = "p k b -> p (k b)"
                dve.wait_ge(x_hi_done, count("TX", ("T", t, q)))
                nc.vector.tensor_tensor(x_lo[:, t % XS, first:first + n, :].rearrange(flat),
                                        ps_x[bank(("T", t, q))][:, 0:n * P],
                                        x_hi[:, t % XS, first:first + n, :].rearrange(flat),
                                        ALU.subtract).then_inc(x_lo_done, 1)

            def pair_operands(t, q):
                first, n = BATCHES[q]
                if q == 0 and t >= 1:
                    dve.wait_ge(gram_made, GBANKS * t)
                dve.wait_ge(x_lo_done, count("TX", ("T", t, q)))
                for par in range(2):
                    f = slice(2 * first + par, 2 * (first + n), 2)
                    part = slice(K * par, K * (par + 1))
                    nc.vector.tensor_copy(pair_u[K:2 * K, f, :], x_lo[part, t % XS, first:first + n, :])
                    last = nc.vector.tensor_copy(pair_v[K:2 * K, f, :],
                                                 x_hi[part, t % XS, first:first + n, :])
                last.then_inc(pairs_dve, 1)

            def read_pairs(t, q):
                if q % 2 == 1:
                    dve.wait_ge(gram_made, GBANKS * t + q + 1)
                    nc.vector.tensor_copy(gram[:, GB * q:GB * (q + 1), :].rearrange("i b j -> i (b j)"),
                                          ps_g[q % 2][0:FIELDS, 0:GB * FIELDS]).then_inc(gram_dve, 1)

            def make_tail(t):
                if t == 0:
                    dve.wait_ge(dense_in, 16)
                dve.wait_ge(rows_done, 2 * t + 1)
                nc.vector.tensor_copy(tail[:, PAIRS:PAIRS + DENSE], dense[:, t, :])
                dve.wait_ge(rows_done, 2 * t + 2)
                for i in range(FIELDS - 1):
                    last = nc.vector.tensor_tensor(tail[:, row_of(i):row_of(i + 1)],
                                                   square[:, i, i + 1:FIELDS],
                                                   square[:, i + 1:FIELDS, i], ALU.add)
                last.then_inc(tail_done, 1)

            def low_tail(t):
                flat = "p k b -> p (k b)"
                dve.wait_ge(x_hi_done, count("TX", ("X", t, 0)))
                nc.vector.tensor_tensor(x_lo[:, t % XS, FP:KT, :].rearrange(flat),
                                        ps_x[bank(("X", t, 0))][:, 0:TT * P],
                                        x_hi[:, t % XS, FP:KT, :].rearrange(flat),
                                        ALU.subtract).then_inc(x_lo_done, 1)

            def second_layer(n):
                h = n % HALVES
                if n == 0:
                    dve.wait_ge(w2_in, 32)
                for c, w in enumerate(CW):
                    for b in range(GROUP):
                        j = GROUP * c + b
                        if j < len(acc) - 1:
                            dve.wait_ge(acc_made, (len(acc) - 1) * n + j + 1)
                        else:
                            dve.wait_ge(w_used, last_of(n) + 1)
                        if len(acc) * n + j >= 2:
                            dve.wait_ge(acc_read, len(acc) * n + j - 1)
                        at, col = sum(CW[:c]), 4 * (n // HALVES * GROUP + b) + 2 * h + c
                        nc.vector.scalar_tensor_tensor(
                            out=weighed[:, j % 2, 0:w], in0=acc[j][:, 0:w], scalar=0.0,
                            in1=w2b[:, h, at:at + w], op0=ALU.max, op1=ALU.mult,
                            accum_out=parts[:, col:col + 1]).then_inc(acc_read, 1)

            PARTS = {"T": low_z, "O": pair_operands, "G": read_pairs, "R": lambda t, _: make_tail(t),
                     "X": lambda t, _: low_tail(t)}
            for m in range(2):
                split_piece(m)
            for u in range(FIRST, TURNS):
                for m in ahead(u):
                    split_piece(m)
                if u >= 0 and u == last_of(TURN[u][0]):
                    second_layer(TURN[u][0])
                for kind, t, q in AFTER.get(u, []):
                    PARTS[kind](t, q)
            dve.wait_ge(acc_read, len(acc) * STEPS)
            nc.vector.tensor_reduce(out=logits[:], in_=parts[:].rearrange("p (t c) -> p t c", c=4),
                                    axis=AX.X, op=ALU.add).then_inc(sum_done, 1)


_INS = ['r_x_dense', 'r_x_sparse', 'L0_rec_emb_tables', 'L0_rec_w1', 'L0_rec_b1', 'L0_rec_w2', 'L0_rec_b2']
_OUTS = [((1024, 1), 'float32')]


def kernel(**inputs):
    import numpy as _np
    import concourse.bacc as _bacc
    from concourse import mybir as _mybir
    from concourse.bass_utils import run_bass_kernel_spmd as _run

    nc = _bacc.Bacc("TRN2", target_bir_lowering=False, num_devices=1)
    arrays, args = {}, []
    for name in _INS:
        a = _np.ascontiguousarray(inputs[name])
        arrays[f"in_{name}_dram"] = a
        args.append(nc.dram_tensor(f"in_{name}_dram", a.shape, _mybir.dt.from_np(a.dtype), kind="ExternalInput").ap())
    for i, (shape, dtype) in enumerate(_OUTS):
        dt = _mybir.dt.from_np(_np.dtype(dtype))
        args.append(nc.dram_tensor(f"out_{i}_dram", shape, dt, kind="ExternalOutput").ap())
    product_interaction_mlp_kernel(nc, *args)
    r = _run(nc, [arrays], core_ids=[0])
    return r.results[0]["out_0_dram"]
```

```python
import concourse.bass as bass
from concourse import mybir
from contextlib import ExitStack


def product_interaction_mlp_kernel(nc, x_dense, x_sparse, emb, w1, b1, w2, b2, out):
    fp32 = mybir.dt.float32
    f32r = mybir.dt.float32r
    i32 = mybir.dt.int32
    ALU = mybir.AluOpType
    ACT = mybir.ActivationFunctionType
    AX = mybir.AxisListType

    P = 128
    BATCH, DENSE = x_dense.shape
    FIELDS, VOCAB, K = emb.shape
    HID = w1.shape[0]
    TILES = BATCH // P
    GROUP = 2
    PAIRS = FIELDS * (FIELDS - 1) // 2
    FP = FIELDS // 2
    TAIL = PAIRS + DENSE + 1
    TT = -(-TAIL // P)
    KT = FP + TT
    LAST = TAIL - (TT - 1) * P
    HALVES = 2
    CW = [502, 500]
    HW = sum(CW)
    HSTEP = HID - HW
    BATCHES = [(0, 3), (3, 4), (7, 4), (11, FP - 11)]
    GB = 16
    GBANKS = P // GB
    RAW = 4
    SPL = 6
    ALONE = 11
    WARM_UP = 48
    LEAD = 4
    XS = 4
    RR = FIELDS // 2

    STEPS = HALVES * TILES // GROUP

    TURN = [(0, k, [t]) for t in range(GROUP) for k in range(ALONE)]
    TURN += [(0, k, list(range(GROUP))) for k in range(ALONE, KT)]
    for n in range(1, STEPS):
        TURN += [(n, k, [n // HALVES * GROUP + b for b in range(GROUP)]) for k in range(KT)]
    TURNS = len(TURN)

    PLAN = [
        ([-1, 2, 6, 10], [0.5, 3.5, 7.5, 10.1],
         [10.6, 10.6, 10.6, 10.6, 10.6, 10.6, 10.6, 10.6], [12.5], [13.5]),
        ([10.8, 13, 16, 19], [11.6, 14.5, 18.5, 21.1],
         [21.5, 21.5, 21.5, 21.5, 21.6, 21.6, 21.6, 21.6], [22.8], [23.7]),
        ([22.8, 22.9, 24.9, 26.9], [24.3, 26, 27, 29],
         [30.1, 30.1, 31.1, 31.1, 32.1, 32.1, 32.1, 32.1], [33.1], [35.5]),
        ([37, 37.5, 40.5, 41.5], [40, 40, 42, 43],
         [44.5, 44.5, 45.5, 45.5, 46.5, 46.5, 47.5, 47.5], [48.5], [51]),
        ([50, 52, 54, 56], [51.5, 53.5, 55.5, 57.5],
         [58.5, 58.5, 59.5, 59.5, 60.5, 60.5, 61.5, 61.5], [62.5], [63.5]),
        ([64, 66, 68, 70], [65.5, 67.5, 69.5, 71.5],
         [72.5, 72.5, 73.5, 73.5, 74.5, 74.5, 75.5, 75.5], [76.9], [79.5]),
        ([79, 81, 83, 85], [80.5, 82.5, 84.5, 86.5],
         [87.5, 87.5, 88.5, 88.5, 89.5, 89.5, 90.5, 90.5], [91.5], [92.5]),
        ([92, 94, 96, 98], [93.5, 95.5, 97.5, 99.4],
         [100.6, 100.6, 101.6, 101.6, 102.6, 102.6, 103.6, 103.6], [104.5], [105.5]),
    ]
    WARM = [(2.1, 5), (6.1, 5), (10.2, 9), (12.2, 1), (13.1, 5), (17.1, 4), (20.1, 6), (21.1, 5),
            (23.2, 8)]
    plan = [(int(10 * u + 0.5), t, "TOGRX".index(kind), q, kind)
            for t, tile_plan in enumerate(PLAN) for kind, places in zip("TOGRX", tile_plan)
            for q, u in enumerate(places)]
    plan += [(int(10 * u + 0.5), TILES + i, len("TOGRX"), n, "W") for i, (u, n) in enumerate(WARM)]
    EARLY, LATE = {}, {}
    for u, t, _, q, kind in sorted(plan):
        (EARLY if u % 10 < 5 else LATE).setdefault(u // 10, []).append((kind, t, q))
    FIRST = -1
    ORDER = [e for u in range(FIRST, TURNS) for e in EARLY.get(u, []) + LATE.get(u, [])]

    def count(kinds, event):
        return sum(e[0] in kinds for e in ORDER[:ORDER.index(event) + 1])

    USES = [(*e, j) for e in ORDER if e[0] != "O" for j in range(2 if e[0] == "R" else 1)]
    BANKS = 4

    def bank(event, j=0):
        return side[USES.index((*event, j)) % BANKS]

    emb_rows = emb.rearrange("f v k -> (f v) k")

    def row_of(i):
        return sum(FIELDS - 1 - m for m in range(i))

    with ExitStack() as ctx:
        def sb(name, shape, dt):
            return ctx.enter_context(nc.sbuf_tensor(name, shape, dt))

        def pb(name):
            return ctx.enter_context(nc.psum_tensor(name, [P, 512], fp32))

        def sem(name):
            return ctx.enter_context(nc.semaphore(name))

        idx = sb("idx", [P, TILES, FIELDS], i32)
        wrap = sb("wrap", [P, TILES, FIELDS], i32)
        base = sb("base", [P, TILES, FIELDS], i32)
        ident = sb("ident", [P, P], fp32)
        dense = sb("dense", [P, TILES, DENSE], fp32)
        w2b = sb("w2b", [P, HALVES, HW], fp32)
        b2b = sb("b2b", [TILES, 1], fp32)
        z = sb("z", [P, 2, FIELDS * K], fp32)
        x_hi = sb("x_hi", [P, XS, KT, P], f32r)
        x_lo = sb("x_lo", [P, XS, KT, P], f32r)
        pair_u = sb("pair_u", [P, FIELDS, P], f32r)
        pair_v = sb("pair_v", [P, FIELDS, P], f32r)
        gram = sb("gram", [FIELDS, P, FIELDS], fp32)
        square = sb("square", [P, FIELDS, FIELDS], fp32)
        tail = sb("tail", [P, TT * P], fp32)
        w_raw = sb("w_raw", [P, RAW, HW], fp32)
        w_hi = sb("w_hi", [P, SPL, HW], f32r)
        w_lo = sb("w_lo", [P, SPL, HW], f32r)
        weighed = sb("weighed", [P, 2, 512], fp32)
        parts = sb("parts", [P, TILES * 2 * HALVES], fp32)
        logits = sb("logits", [P, TILES], fp32)
        y = sb("y", [TILES, P], fp32)

        acc = [pb(f"acc{j}") for j in range(4)]
        side = [pb(f"side{j}") for j in range(BANKS)]

        idx_in = sem("idx_in")
        dense_in = sem("dense_in")
        w2_in = sem("w2_in")
        b2_in = sem("b2_in")
        w_in = [sem(f"w_in{j}") for j in range(RAW)]
        base_done = sem("base_done")
        ident_zero = sem("ident_zero")
        ident_done = sem("ident_done")
        idx_step = sem("idx_step")
        idx_done = sem("idx_done")
        w2_zero = sem("w2_zero")
        gathered = [[sem(f"gathered{z}_{q}") for q in range(len(BATCHES))] for z in range(2)]
        transposed = sem("transposed")
        x_hi_done = sem("x_hi_done")
        x_lo_done = sem("x_lo_done")
        pairs_act = sem("pairs_act")
        pairs_dve = sem("pairs_dve")
        gram_made = sem("gram_made")
        gram_act = sem("gram_act")
        gram_dve = sem("gram_dve")
        rows_made = sem("rows_made")
        rows_done = sem("rows_done")
        tail_done = sem("tail_done")
        w_hi_done = sem("w_hi_done")
        w_lo_done = sem("w_lo_done")
        w_used = sem("w_used")
        acc_made = sem("acc_made")
        acc_read = sem("acc_read")
        sum_done = sem("sum_done")
        y_made = sem("y_made")
        y_done = sem("y_done")
        out_done = sem("out_done")

        block = ctx.enter_context(nc.Block())

        def ahead(u):
            return [m for m in range(2, TURNS) if max(m - LEAD, 0) == u]

        def last_of(n):
            return max(u for u in range(TURNS) if TURN[u][0] == n)

        def gram_counts(n):
            return (n + 1) // 2, n // 2

        def raw_count(m):
            return 16 * sum(3 if TURN[i][1] == KT - 1 else 1 for i in range(m % RAW, m + 1, RAW))

        @block.sync
        def _(sp):
            sp.dma_start(idx[:], x_sparse.rearrange("(t p) f -> p t f", p=P)).then_inc(idx_in, 16)

            def load_piece(m):
                k, h = TURN[m][1], TURN[m][0] % HALVES
                cols, slot = slice(h * HSTEP, h * HSTEP + HW), m % RAW
                if m >= RAW:
                    sp.wait_ge(w_lo_done, m - RAW + 1)
                if k < KT - 1:
                    r = DENSE + P * k
                    sp.dma_start(w_raw[:, slot, :], w1[r:r + P, cols]).then_inc(w_in[slot], 16)
                else:
                    n = PAIRS - (TT - 1) * P
                    sp.dma_start(w_raw[0:n, slot, :], w1[HID - n:HID, cols]).then_inc(w_in[slot], 16)
                    sp.dma_start(w_raw[n:n + DENSE, slot, :], w1[0:DENSE, cols]).then_inc(w_in[slot], 16)
                    sp.dma_start(w_raw[n + DENSE:LAST, slot, :],
                                 b1[cols].unsqueeze(0)).then_inc(w_in[slot], 16)

            for m in range(LEAD):
                if m >= 2:
                    sp.wait_ge(w_lo_done, m - 1)
                load_piece(m)
            sp.dma_start(dense[:], x_dense.rearrange("(t p) d -> p t d", p=P)).then_inc(dense_in, 16)
            sp.wait_ge(w2_zero, 1)
            for h in range(HALVES):
                o = 2 if h else 0
                sp.dma_start(w2b[:, h, o:HW],
                             w2[h * HSTEP + o:h * HSTEP + HW, :].rearrange("n o -> o n")
                             .broadcast_to([P, HW - o])).then_inc(w2_in, 16)
            sp.dma_start(b2b[:], b2.unsqueeze(0).broadcast_to([TILES, 1])).then_inc(b2_in, 16)
            for m in range(LEAD, TURNS):
                load_piece(m)
            sp.wait_ge(y_done, 1)
            sp.dma_start(out.rearrange("(t p) o -> t (p o)", p=P), y[:]).then_inc(out_done, 16)
            sp.wait_ge(out_done, 16)

        @block.gpsimd
        def _(pool):
            nc.gpsimd.iota(base[:], pattern=[[0, TILES], [VOCAB, FIELDS]], base=0,
                           channel_multiplier=0).then_inc(base_done, 1)
            nc.gpsimd.memset(ident[:], 0.0).then_inc(ident_zero, 1)
            pool.wait_ge(ident_zero, 1)
            nc.gpsimd.affine_select(out=ident[:], in_=ident[:], compare_op=ALU.not_equal, fill=1.0, base=0,
                                    pattern=[[-1, P]], channel_multiplier=1).then_inc(ident_done, 1)
            pool.wait_ge(idx_done, 1)
            for t in range(TILES):
                for q, (first, n) in enumerate(BATCHES):
                    if t >= 2:
                        pool.wait_ge(transposed, count("TX", ("T", t - 2, q)))
                    for f in range(2 * first, 2 * (first + n)):
                        pool.indirect_dma_start(
                            out=z[:, t % 2, K * f:K * (f + 1)], out_offset=None, in_=emb_rows,
                            in_offset=bass.IndirectOffsetOnAxis(ap=idx[:, t, f:f + 1], axis=0),
                        ).then_inc(gathered[t % 2][q], 16)

        @block.tensor
        def _(pe):
            def bank_free(event, j=0):
                u = USES.index((*event, j))
                if u >= BANKS:
                    kind, t, q, i = USES[u - BANKS]
                    if kind == "R":
                        pe.wait_ge(rows_done, 2 * t + 1 + i)
                    elif kind == "G" and q % 2 == 0:
                        pe.wait_ge(gram_act, gram_counts(GBANKS * t + q + 1)[0])
                    elif kind == "G":
                        pe.wait_ge(gram_dve, gram_counts(GBANKS * t + q + 1)[1])
                    elif kind in "TX":
                        pe.wait_ge(x_lo_done, count("TX", (kind, t, q)))

            def keep_warm(t, n):
                bank_free(("W", t, n))
                for _ in range(n):
                    nc.tensor.matmul(bank(("W", t, n))[:, 0:P], ident[:], ident[:], start=True, stop=True)

            def transpose_z(t, q):
                first, n = BATCHES[q]
                pe.wait_ge(gathered[t % 2][q], 16 * 2 * n * (t // 2 + 1))
                bank_free(("T", t, q))
                for j in range(n):
                    last = nc.tensor.transpose(bank(("T", t, q))[:, P * j:P * (j + 1)],
                                               z[:, t % 2, P * (first + j):P * (first + j + 1)], ident[:])
                last.then_inc(transposed, 1)

            def pair_products(t, q):
                if q == 0:
                    pe.wait_ge(pairs_act, len(BATCHES) * (t + 1))
                    pe.wait_ge(pairs_dve, len(BATCHES) * (t + 1))
                bank_free(("G", t, q))
                for g in range(GB):
                    s = GB * q + g
                    last = nc.tensor.matmul(bank(("G", t, q))[0:FIELDS, g * FIELDS:(g + 1) * FIELDS],
                                            pair_u[:, :, s], pair_v[:, :, s], start=True, stop=True)
                last.then_inc(gram_made, 1)

            def product_rows(t):
                pe.wait_ge(gram_act, gram_counts(GBANKS * (t + 1))[0])
                pe.wait_ge(gram_dve, gram_counts(GBANKS * (t + 1))[1])
                for j in range(2):
                    bank_free(("R", t, 0), j)
                    for i in range(RR):
                        last = nc.tensor.transpose(
                            bank(("R", t, 0), j)[:, FIELDS * i:FIELDS * (i + 1)],
                            gram[:, :, RR * j + i], ident[0:FIELDS, 0:FIELDS])
                    last.then_inc(rows_made, 1)

            def transpose_tail(t):
                pe.wait_ge(tail_done, t + 1)
                bank_free(("X", t, 0))
                for j in range(TT):
                    last = nc.tensor.transpose(bank(("X", t, 0))[:, P * j:P * (j + 1)],
                                               tail[:, P * j:P * (j + 1)], ident[:])
                last.then_inc(transposed, 1)

            def multiply(m):
                (n, k, tiles), slot = TURN[m], m % SPL
                rows = LAST if k == KT - 1 else P
                event = [("T", q) for q, (first, _) in enumerate(BATCHES) if k == first]
                event += [("X", 0)] if k == FP else []

                def wait_x(done, t):
                    for kind, q in event:
                        pe.wait_ge(done, count("TX", (kind, t, q)))

                def chunk(c, t):
                    j = GROUP * c + t % GROUP
                    cols = slice(sum(CW[:c]), sum(CW[:c + 1]))
                    return j, acc[j][:, 0:CW[c]], w_hi[0:rows, slot, cols], w_lo[0:rows, slot, cols]

                def low_part(c, t):
                    j, o, wh, _ = chunk(c, t)
                    last = nc.tensor.matmul(o, x_lo[0:rows, t % XS, k, :], wh, start=False,
                                            stop=k == KT - 1)
                    if k == KT - 1 and j < len(acc) - 1:
                        last.then_inc(acc_made, 1)
                    return last

                pe.wait_ge(w_hi_done, m + 1)
                pe.wait_ge(w_lo_done, m + 1)
                for c in range(2):
                    for t in tiles:
                        j, o, wh, wl = chunk(c, t)
                        if k == 0 and n >= 1:
                            pe.wait_ge(acc_read, len(acc) * (n - 1) + j + 1)
                        if c == 0:
                            wait_x(x_hi_done, t)
                        hi = x_hi[0:rows, t % XS, k, :]
                        nc.tensor.matmul(o, hi, wh, start=k == 0, stop=False)
                        nc.tensor.matmul(o, hi, wl, start=False, stop=False)
                        if k == KT - 1:
                            last = low_part(c, t)
                if k < KT - 1:
                    for c in range(2):
                        for t in tiles:
                            if c == 0:
                                wait_x(x_lo_done, t)
                            last = low_part(c, t)
                last.then_inc(w_used, 1)

            PARTS = {"T": transpose_z, "G": pair_products, "R": lambda t, _: product_rows(t),
                     "X": lambda t, _: transpose_tail(t), "O": lambda t, q: None, "W": keep_warm}
            pe.wait_ge(ident_done, 1)
            for _ in range(WARM_UP):
                nc.tensor.matmul(side[0][:, 0:P], ident[:], ident[:], start=True, stop=True)
            for u in range(FIRST, TURNS):
                if u >= 0:
                    multiply(u)
                for kind, t, q in EARLY.get(u, []) + LATE.get(u, []):
                    PARTS[kind](t, q)
            pe.wait_ge(sum_done, 1)
            nc.tensor.transpose(side[0][0:TILES, 0:P], logits[:], ident[:]).then_inc(y_made, 1)

        @block.scalar
        def _(act):
            def split_piece(m):
                slot = m % SPL
                rows = LAST if TURN[m][1] == KT - 1 else P
                act.wait_ge(w_in[m % RAW], raw_count(m))
                if m >= SPL:
                    act.wait_ge(w_used, m - SPL + 1)
                nc.scalar.copy(w_hi[0:rows, slot, :], w_raw[0:rows, m % RAW, :]).then_inc(w_hi_done, 1)

            def high_z(t, q):
                first, n = BATCHES[q]
                act.wait_ge(transposed, count("TX", ("T", t, q)))
                nc.scalar.copy(x_hi[:, t % XS, first:first + n, :].rearrange("p k b -> p (k b)"),
                               bank(("T", t, q))[:, 0:n * P]).then_inc(x_hi_done, 1)

            def pair_operands(t, q):
                first, n = BATCHES[q]
                if q == 0 and t >= 1:
                    act.wait_ge(gram_made, GBANKS * t)
                act.wait_ge(x_hi_done, count("TX", ("T", t, q)))
                for par in range(2):
                    f = slice(2 * first + par, 2 * (first + n), 2)
                    high = x_hi[K * par:K * (par + 1), t % XS, first:first + n, :].bitcast(fp32)
                    nc.scalar.mul(pair_v[0:K, f, :], high, 0.5)
                    last = nc.scalar.copy(pair_u[0:K, f, :], high)
                last.then_inc(pairs_act, 1)

            def read_pairs(t, q):
                if q % 2 == 0:
                    act.wait_ge(gram_made, GBANKS * t + q + 1)
                    nc.scalar.copy(gram[:, GB * q:GB * (q + 1), :].rearrange("i b j -> i (b j)"),
                                   bank(("G", t, q))[0:FIELDS, 0:GB * FIELDS]).then_inc(gram_act, 1)

            def read_rows(t):
                for j in range(2):
                    act.wait_ge(rows_made, 2 * t + j + 1)
                    nc.scalar.copy(square[:, RR * j:RR * (j + 1), :].rearrange("p i j -> p (i j)"),
                                   bank(("R", t, 0), j)[:, 0:RR * FIELDS]).then_inc(rows_done, 1)

            def high_tail(t):
                act.wait_ge(transposed, count("TX", ("X", t, 0)))
                nc.scalar.copy(x_hi[:, t % XS, FP:KT, :].rearrange("p k b -> p (k b)"),
                               bank(("X", t, 0))[:, 0:TT * P]).then_inc(x_hi_done, 1)

            PARTS = {"T": high_z, "O": pair_operands, "G": read_pairs, "R": lambda t, _: read_rows(t),
                     "W": lambda t, q: None,
                     "X": lambda t, _: high_tail(t)}
            for m in range(2):
                split_piece(m)
            for u in range(FIRST, TURNS):
                for kind, t, q in EARLY.get(u, []):
                    PARTS[kind](t, q)
                for m in ahead(u):
                    split_piece(m)
                for kind, t, q in LATE.get(u, []):
                    PARTS[kind](t, q)
            act.wait_ge(b2_in, 16)
            act.wait_ge(y_made, 1)
            nc.scalar.activation(y[:], side[0][0:TILES, 0:P], ACT.Sigmoid, bias=b2b[:]).then_inc(y_done, 1)

        @block.vector
        def _(dve):
            dve.wait_ge(idx_in, 16)
            nc.vector.tensor_scalar(wrap[:], idx[:], 0, VOCAB, ALU.is_lt, ALU.mult).then_inc(idx_step, 1)
            dve.wait_ge(idx_step, 1)
            nc.vector.tensor_tensor(idx[:], idx[:], wrap[:], ALU.add).then_inc(idx_step, 1)
            dve.wait_ge(idx_step, 2)
            nc.vector.tensor_scalar(idx[:], idx[:], VOCAB - 1, 0, ALU.min, ALU.max).then_inc(idx_step, 1)
            dve.wait_ge(idx_step, 3)
            dve.wait_ge(base_done, 1)
            nc.vector.tensor_tensor(idx[:], idx[:], base[:], ALU.add).then_inc(idx_done, 1)
            nc.vector.memset(tail[:, TAIL:TT * P], 0.0)
            nc.vector.memset(tail[:, TAIL - 1:TAIL], 1.0)
            nc.vector.memset(w2b[:, 1, 0:2], 0.0).then_inc(w2_zero, 1)

            def split_piece(m):
                slot = m % SPL
                rows = LAST if TURN[m][1] == KT - 1 else P
                dve.wait_ge(w_hi_done, m + 1)
                nc.vector.tensor_tensor(w_lo[0:rows, slot, :], w_raw[0:rows, m % RAW, :],
                                        w_hi[0:rows, slot, :], ALU.subtract).then_inc(w_lo_done, 1)

            def low_z(t, q):
                first, n = BATCHES[q]
                flat = "p k b -> p (k b)"
                dve.wait_ge(x_hi_done, count("TX", ("T", t, q)))
                nc.vector.tensor_tensor(x_lo[:, t % XS, first:first + n, :].rearrange(flat),
                                        bank(("T", t, q))[:, 0:n * P],
                                        x_hi[:, t % XS, first:first + n, :].rearrange(flat),
                                        ALU.subtract).then_inc(x_lo_done, 1)

            def pair_operands(t, q):
                first, n = BATCHES[q]
                if q == 0 and t >= 1:
                    dve.wait_ge(gram_made, GBANKS * t)
                dve.wait_ge(x_lo_done, count("TX", ("T", t, q)))
                for par in range(2):
                    f = slice(2 * first + par, 2 * (first + n), 2)
                    part = slice(K * par, K * (par + 1))
                    nc.vector.tensor_copy(pair_u[K:2 * K, f, :], x_lo[part, t % XS, first:first + n, :])
                    last = nc.vector.tensor_copy(pair_v[K:2 * K, f, :],
                                                 x_hi[part, t % XS, first:first + n, :])
                last.then_inc(pairs_dve, 1)

            def read_pairs(t, q):
                if q % 2 == 1:
                    dve.wait_ge(gram_made, GBANKS * t + q + 1)
                    nc.vector.tensor_copy(gram[:, GB * q:GB * (q + 1), :].rearrange("i b j -> i (b j)"),
                                          bank(("G", t, q))[0:FIELDS, 0:GB * FIELDS]).then_inc(gram_dve, 1)

            def make_tail(t):
                if t == 0:
                    dve.wait_ge(dense_in, 16)
                dve.wait_ge(rows_done, 2 * t + 1)
                nc.vector.tensor_copy(tail[:, PAIRS:PAIRS + DENSE], dense[:, t, :])
                dve.wait_ge(rows_done, 2 * t + 2)
                for i in range(FIELDS - 1):
                    last = nc.vector.tensor_tensor(tail[:, row_of(i):row_of(i + 1)],
                                                   square[:, i, i + 1:FIELDS],
                                                   square[:, i + 1:FIELDS, i], ALU.add)
                last.then_inc(tail_done, 1)

            def low_tail(t):
                flat = "p k b -> p (k b)"
                dve.wait_ge(x_hi_done, count("TX", ("X", t, 0)))
                nc.vector.tensor_tensor(x_lo[:, t % XS, FP:KT, :].rearrange(flat),
                                        bank(("X", t, 0))[:, 0:TT * P],
                                        x_hi[:, t % XS, FP:KT, :].rearrange(flat),
                                        ALU.subtract).then_inc(x_lo_done, 1)

            def second_layer(n):
                h = n % HALVES
                if n == 0:
                    dve.wait_ge(w2_in, 32)
                for c, w in enumerate(CW):
                    for b in range(GROUP):
                        j = GROUP * c + b
                        if j < len(acc) - 1:
                            dve.wait_ge(acc_made, (len(acc) - 1) * n + j + 1)
                        else:
                            dve.wait_ge(w_used, last_of(n) + 1)
                        if len(acc) * n + j >= 2:
                            dve.wait_ge(acc_read, len(acc) * n + j - 1)
                        at, col = sum(CW[:c]), 4 * (n // HALVES * GROUP + b) + 2 * h + c
                        nc.vector.scalar_tensor_tensor(
                            out=weighed[:, j % 2, 0:w], in0=acc[j][:, 0:w], scalar=0.0,
                            in1=w2b[:, h, at:at + w], op0=ALU.max, op1=ALU.mult,
                            accum_out=parts[:, col:col + 1]).then_inc(acc_read, 1)

            PARTS = {"T": low_z, "O": pair_operands, "G": read_pairs, "R": lambda t, _: make_tail(t),
                     "W": lambda t, q: None,
                     "X": lambda t, _: low_tail(t)}
            for m in range(2):
                split_piece(m)
            for u in range(FIRST, TURNS):
                if u >= 0 and u == last_of(TURN[u][0]):
                    second_layer(TURN[u][0])
                for kind, t, q in EARLY.get(u, []):
                    PARTS[kind](t, q)
                for m in ahead(u):
                    split_piece(m)
                for kind, t, q in LATE.get(u, []):
                    PARTS[kind](t, q)
            dve.wait_ge(acc_read, len(acc) * STEPS)
            nc.vector.tensor_reduce(out=logits[:], in_=parts[:].rearrange("p (t c) -> p t c", c=4),
                                    axis=AX.X, op=ALU.add).then_inc(sum_done, 1)


_INS = ['r_x_dense', 'r_x_sparse', 'L0_rec_emb_tables', 'L0_rec_w1', 'L0_rec_b1', 'L0_rec_w2', 'L0_rec_b2']
_OUTS = [((1024, 1), 'float32')]


def kernel(**inputs):
    import numpy as _np
    import concourse.bacc as _bacc
    from concourse import mybir as _mybir
    from concourse.bass_utils import run_bass_kernel_spmd as _run

    nc = _bacc.Bacc("TRN2", target_bir_lowering=False, num_devices=1)
    arrays, args = {}, []
    for name in _INS:
        a = _np.ascontiguousarray(inputs[name])
        arrays[f"in_{name}_dram"] = a
        args.append(nc.dram_tensor(f"in_{name}_dram", a.shape, _mybir.dt.from_np(a.dtype), kind="ExternalInput").ap())
    for i, (shape, dtype) in enumerate(_OUTS):
        dt = _mybir.dt.from_np(_np.dtype(dtype))
        args.append(nc.dram_tensor(f"out_{i}_dram", shape, dt, kind="ExternalOutput").ap())
    product_interaction_mlp_kernel(nc, *args)
    r = _run(nc, [arrays], core_ids=[0])
    return r.results[0]["out_0_dram"]
```
